# Optimizing a Trainium2 kernel written in Bass

```python
import numpy as np
import jax
import jax.numpy as jnp

def _softmax(x, axis=-1):
    return jax.nn.softmax(x, axis=axis)

def _gelu(x):
    return jax.nn.gelu(x, approximate=True)

def _silu(x):
    return jax.nn.silu(x)

def _sigmoid(x):
    return jax.nn.sigmoid(x)

def _layernorm(x, axis=-1, eps=1e-05):
    m = jnp.mean(x, axis=axis, keepdims=True)
    v = jnp.var(x, axis=axis, keepdims=True)
    return (x - m) / jnp.sqrt(v + eps)

def _scatter_add(tgt, idx, src, axis=0):
    return tgt.at[idx].add(src)

def _segment_sum(src, seg, n):
    return jax.ops.segment_sum(src, seg, n)
kernel_name = 'mk_lm_tower_d1_tok_ids2048_r4_a5365d'

def setup_inputs(seed: int=0):
    np.random.seed(seed)
    _w = jnp.asarray

    def _rec_inputs():
        import jax
        import jax.numpy as jnp
        _rk = jax.random.key(seed)
        x = jax.random.randint(jax.random.fold_in(_rk, 1), (2, 1024), 0, 12096, jnp.int32)
        return x
    x = _rec_inputs()

    def _L0_tok_setup():
        import jax, jax.numpy as jnp
        import numpy as np
        ADDED_TOKENS_OFFSET = 8000
        VQGAN_START = 8000
        VQGAN_END = 12096
        IMAGE_TOKEN_OFFSET = 8000
        VOCAB = 8000
        VQ_VOCAB = 4096
        EMBED_DIM = 512
        VQ_DIM = 64
        B, S = (8, 1024)
        key = jax.random.key(seed)
        k1, k2, k3, k4 = jax.random.split(key, 4)
        x = jax.random.randint(k1, (B, S), 0, VQGAN_END, dtype=jnp.int64 if jax.config.jax_enable_x64 else jnp.int32)
        tok_emb = jax.random.normal(k2, (VOCAB, EMBED_DIM), dtype=jnp.float32) * 0.02
        codebook = jax.random.normal(k3, (VQ_VOCAB, VQ_DIM), dtype=jnp.float32) * 0.02
        proj_w = jax.random.normal(k4, (EMBED_DIM, VQ_DIM), dtype=jnp.float32) * 0.02
        return {'x': x, 'tok_emb': tok_emb, 'codebook': codebook, 'proj_w': proj_w}
    _L0_tok_all = _L0_tok_setup()
    _L0_tok_in = {k: v for k, v in _L0_tok_all.items() if k in ('tok_emb', 'codebook', 'proj_w')}
    del _L0_tok_all

    def _L0_attn_setup():
        import jax, jax.numpy as jnp
        import numpy as np
        C_GATE = 8.0
        key = jax.random.key(seed)
        k1, k2, k3 = jax.random.split(key, 3)
        bsz, seqlen, emb_dim, head_dim = (4, 1024, 512, 128)
        x = jax.random.normal(k1, (bsz, seqlen, emb_dim), dtype=jnp.float32)
        W_in = jax.random.normal(k2, (2 * emb_dim, emb_dim), dtype=jnp.float32) * emb_dim ** (-0.5)
        a_param = jax.random.normal(k3, (head_dim,), dtype=jnp.float32)
        return {'x': x, 'W_in': W_in, 'a_param': a_param}
    _L0_attn_all = _L0_attn_setup()
    _L0_attn_in = {k: v for k, v in _L0_attn_all.items() if k in ('W_in', 'a_param')}
    del _L0_attn_all

    def _L0_ffn_setup():
        import jax, jax.numpy as jnp
        import numpy as np
        B, S, H = (4, 512, 512)
        E = 8
        F = H // E
        TOPK = 2
        LORA_R = 16
        LORA_SCALE = 1.0
        key = jax.random.key(seed)
        ks = jax.random.split(key, 7)
        x = jax.random.normal(ks[0], (B, S, H), dtype=jnp.float32)
        G = jax.random.normal(ks[1], (H, E), dtype=jnp.float32)
        gate_w = jax.random.normal(ks[2], (E, F, H), dtype=jnp.float32) * np.float32(np.sqrt(2.0 / H))
        up_w = jax.random.normal(ks[3], (E, F, H), dtype=jnp.float32) * np.float32(np.sqrt(2.0 / H))
        down_w = jax.random.normal(ks[4], (E, H, F), dtype=jnp.float32) * np.float32(np.sqrt(2.0 / F))
        lora_A = jax.random.normal(ks[5], (E, LORA_R, H), dtype=jnp.float32) * np.float32(np.sqrt(2.0 / H))
        lora_B = jax.random.normal(ks[6], (E, H, LORA_R), dtype=jnp.float32) * np.float32(np.sqrt(2.0 / LORA_R))
        return {'x': x, 'G': G, 'gate_w': gate_w, 'up_w': up_w, 'down_w': down_w, 'lora_A': lora_A, 'lora_B': lora_B}
    _L0_ffn_all = _L0_ffn_setup()
    _L0_ffn_in = {k: v for k, v in _L0_ffn_all.items() if k in ('G', 'gate_w', 'up_w', 'down_w', 'lora_A', 'lora_B')}
    del _L0_ffn_all
    return {'x': x, 'L0_tok_tok_emb': _L0_tok_in['tok_emb'], 'L0_tok_codebook': _L0_tok_in['codebook'], 'L0_tok_proj_w': _L0_tok_in['proj_w'], 'L0_attn_W_in': _L0_attn_in['W_in'], 'L0_attn_a_param': _L0_attn_in['a_param'], 'L0_ffn_G': _L0_ffn_in['G'], 'L0_ffn_gate_w': _L0_ffn_in['gate_w'], 'L0_ffn_up_w': _L0_ffn_in['up_w'], 'L0_ffn_down_w': _L0_ffn_in['down_w'], 'L0_ffn_lora_A': _L0_ffn_in['lora_A'], 'L0_ffn_lora_B': _L0_ffn_in['lora_B']}

def reference(x, L0_tok_tok_emb, L0_tok_codebook, L0_tok_proj_w, L0_attn_W_in, L0_attn_a_param, L0_ffn_G, L0_ffn_gate_w, L0_ffn_up_w, L0_ffn_down_w, L0_ffn_lora_A, L0_ffn_lora_B):
    import jax
    import jax.numpy as jnp

    def _L0_tok_ref(x, tok_emb, codebook, proj_w):
        import jax, jax.numpy as jnp
        import numpy as np
        ADDED_TOKENS_OFFSET = 8000
        VQGAN_START = 8000
        VQGAN_END = 12096
        IMAGE_TOKEN_OFFSET = 8000
        VOCAB = 8000
        VQ_VOCAB = 4096
        EMBED_DIM = 512
        VQ_DIM = 64
        B, S = (8, 1024)
        text_mask = (x >= 0) & (x < ADDED_TOKENS_OFFSET)
        image_mask = (x >= VQGAN_START) & (x < VQGAN_END)
        text_tokens = jnp.where(text_mask, x, 0)
        image_tokens = jnp.maximum(jnp.where(image_mask, x, 0) - IMAGE_TOKEN_OFFSET, 0)
        text_embeddings = tok_emb[text_tokens]
        image_latents = codebook[image_tokens]
        image_embeddings = jnp.einsum('bsq,dq->bsd', image_latents, proj_w)
        out = jnp.where(text_mask[..., None], text_embeddings, jnp.where(image_mask[..., None], image_embeddings, 0.0))
        return out

    def _L0_attn_ref(x, W_in, a_param):
        import jax, jax.numpy as jnp
        import numpy as np
        C_GATE = 8.0
        bsz, seqlen, emb_dim = x.shape
        head_dim = a_param.shape[0]
        nb_heads = emb_dim // head_dim
        gates = jnp.einsum('bse,fe->bsf', x, W_in)
        gate_x = jax.nn.sigmoid(gates[..., :emb_dim])
        gate_a = jax.nn.sigmoid(gates[..., emb_dim:])
        a_full = jnp.tile(jax.nn.softplus(a_param), nb_heads)
        log_a = -C_GATE * gate_a * a_full
        a = jnp.exp(log_a)
        multiplier = jnp.sqrt(1.0 - jnp.exp(2.0 * log_a))
        b = multiplier * gate_x * x

        def combine(c1, c2):
            a1, b1 = c1
            a2, b2 = c2
            return (a1 * a2, a2 * b1 + b2)
        _, h = jax.lax.associative_scan(combine, (a, b), axis=1)
        return h

    def _L0_ffn_ref(x, G, gate_w, up_w, down_w, lora_A, lora_B):
        import jax, jax.numpy as jnp
        import numpy as np
        B, S, H = (4, 512, 512)
        E = 8
        F = H // E
        TOPK = 2
        LORA_R = 16
        LORA_SCALE = 1.0
        scores = jax.nn.softmax(jnp.einsum('bsh,he->bse', x, G), axis=-1)
        value, indices = jax.lax.top_k(scores, TOPK)
        onehot = jax.nn.one_hot(indices, E, dtype=value.dtype)
        w = jnp.einsum('bsk,bske->bse', value, onehot)
        gate = jax.nn.silu(jnp.einsum('bsh,efh->bsef', x, gate_w))
        up = jnp.einsum('bsh,efh->bsef', x, up_w)
        gated = gate * up
        out = jnp.einsum('bsef,bse,ehf->bsh', gated, w, down_w)
        lr = jnp.einsum('bsh,erh->bser', x, lora_A)
        out = out + LORA_SCALE * jnp.einsum('bser,bse,ehr->bsh', lr, w, lora_B)
        return out
    h = _L0_tok_ref(x, L0_tok_tok_emb, L0_tok_codebook, L0_tok_proj_w)
    h = h + _L0_attn_ref(_layernorm(h, axis=-1), L0_attn_W_in, L0_attn_a_param)
    h = h + _L0_ffn_ref(_layernorm(h, axis=-1), L0_ffn_G, L0_ffn_gate_w, L0_ffn_up_w, L0_ffn_down_w, L0_ffn_lora_A, L0_ffn_lora_B)
    return h

_drawn_inputs = setup_inputs


def setup_inputs(seed=0):
    import zlib

    import numpy as np

    out = dict(_drawn_inputs(seed))
    spreads = {}
    factors = {}
    for name, (base, spread) in spreads.items():
        noise = np.random.default_rng([zlib.crc32(name.encode()), seed]).standard_normal(out[name].shape)
        drawn = base * np.exp(spread * noise) if base else spread * noise
        out[name] = jnp.asarray(drawn.astype(out[name].dtype))
    for name, factor in factors.items():
        out[name] = (out[name] * factor).astype(out[name].dtype)
    return out
```

```python
from contextlib import ExitStack

import concourse.bass as bass
from concourse import mybir

F32 = mybir.dt.float32
F32R = mybir.dt.float32r
I32 = mybir.dt.int32
ALU = mybir.AluOpType
ACT = mybir.ActivationFunctionType
X = mybir.AxisListType.X

P = 128
T = 2048
SEQ = 1024
D = 512
BT = 512
NB = T // BT
TT = BT // P
KC = D // P
E = 8
F = 64
R = 16
Q = 64
VOCAB = 8000
VQ = 4096
EPS = 1e-5
GC = KC + 1
LORA = KC
ORDER = (0, 1, 2, LORA, 3)
FW = 4096 + 512 + GC * D
PIECE = 1024
OUT_OF_RANGE = 1 << 20
ROUTE = 21


def tower_program(nc, ids, tok_emb, codebook, proj, w_in, a_param, router, w_ffn,
                  identity, selector, rank, out):
    ctx = ExitStack()
    with ctx:
        def sb(name, shape, dt=F32):
            return ctx.enter_context(nc.sbuf_tensor(name, shape, dt))

        def sem(name):
            return ctx.enter_context(nc.semaphore(name))

        hidden = sb("hidden", [P, T // P, D])
        latents = sb("latents", [P, 2, TT, Q])
        latent_parts = sb("latent_parts", [P, TT, 2 * Q], F32R)
        latent_T = sb("latent_T", [P, BT], F32R)
        proj_hi = sb("proj_hi", [P, D], F32R)
        proj_lo = sb("proj_lo", [P, D], F32R)
        win_hi = sb("win_hi", [P, 2 * KC, KC, P], F32R)
        win_lo = sb("win_lo", [P, 2 * KC, KC, P], F32R)
        ffn_hi = sb("ffn_hi", [P, FW], F32R)
        ffn_lo = sb("ffn_lo", [P, FW], F32R)
        router_raw = sb("router_raw", [P, KC, E])
        router_w = sb("router_w", [P, KC * 2 * E + P], F32R)
        select = sb("select", [2 * E, GC, P], F32R)
        ident = sb("ident", [P, P])
        rank_sb = sb("rank_sb", [P, TT, E])
        xg_hi = sb("xg_hi", [P, GC, BT], F32R)
        xg_lo = sb("xg_lo", [P, GC, BT], F32R)
        x2_hi = sb("x2_hi", [P, KC, BT], F32R)
        x2_lo = sb("x2_lo", [P, KC, BT], F32R)
        chan = sb("chan", [P, KC, BT])
        decay = sb("decay", [P, KC, BT])
        mix = sb("mix", [P, KC, BT])
        normed = sb("normed", [P, 2, D])
        prod = sb("prod", [P, 3, BT])
        carry = sb("carry", [P, KC, 1])
        keep = sb("keep", [P, NB, KC])
        ids_sb = sb("ids_sb", [P, T // P], I32)
        text_idx = sb("text_idx", [P, T // P], I32)
        image_idx = sb("image_idx", [P, T // P], I32)
        idx_tmp = sb("idx_tmp", [P, 2, T // P], I32)
        stats1 = sb("stats1", [P, TT, 6])
        stats2 = sb("stats2", [P, TT, 6])
        moments1 = sb("moments1", [P, TT, 2])
        moments2 = sb("moments2", [P, TT, 2])
        rstd1 = sb("rstd1", [P, TT, 1])
        rstd2 = sb("rstd2", [P, TT, 1])
        minus_half = sb("minus_half", [P, TT, 1])
        quarter = sb("quarter", [P, 1])
        ap_sb = sb("ap_sb", [P, 12])
        route = sb("route", [P, 8, TT, E])
        route1 = sb("route1", [P, 8, TT, 1])
        route_w = sb("route_w", [P, TT, 2 * E], F32R)

        logits_T = prod[0:2 * E, 2, :]
        weights_T = xg_hi[0:2 * E, 3, :]
        proj_raw = chan[:, 0, :]
        select_raw = normed[:, :, :].rearrange("p a b -> p (a b)")[0:2 * E, 0:GC * P]
        router_hi_lo = router_w[:, 0:KC * 2 * E].rearrange("p (k e) -> p k e", k=KC)

        ring = [ctx.enter_context(nc.psum_tensor(f"ring{n}", [P, BT], F32)) for n in range(4)]
        turn = [ctx.enter_context(nc.psum_tensor(f"turn{n}", [P, D], F32)) for n in range(2)]
        rows = [ctx.enter_context(nc.psum_tensor(f"rows{n}", [P, D], F32)) for n in range(2)]

        ids_in, a_in, proj_in = sem("ids_in"), sem("a_in"), sem("proj_in")
        ident_in, small_in = sem("ident_in"), sem("small_in")
        win_in = [sem(f"win_in{n}") for n in range(4)]
        ffn_in = [sem(f"ffn_in{n}") for n in range(7)]
        wait_carrier = sem("wait_carrier")
        latents_in, text_in = sem("latents_in"), sem("text_in")
        latents_in_0 = [sem(f"latents_in_0{h}") for h in range(2)]
        text_in_0 = [sem(f"text_in_0{h}") for h in range(2)]
        stored = sem("stored")
        latents_turned = sem("latents_turned")
        proj_done = sem("proj_done")
        x1_turned = sem("x1_turned")
        x2_turned = sem("x2_turned")
        scan_turned = sem("scan_turned")
        gate_done = sem("gate_done")
        logits_done = sem("logits_done")
        logits_turned = sem("logits_turned")
        weights_turned = sem("weights_turned")
        expert_done = sem("expert_done")
        spread_done = sem("spread_done")
        lora_done = sem("lora_done")
        down_done = sem("down_done")
        proj_hi_ready = sem("proj_hi_ready")
        router_hi_ready = sem("router_hi_ready")
        select_ready = sem("select_ready")
        win_hi_ready = sem("win_hi_ready")
        ffn_hi_ready = sem("ffn_hi_ready")
        soft_act = sem("soft_act")
        latent_T_ready = sem("latent_T_ready")
        x1_hi_ready = sem("x1_hi_ready")
        x2_hi_ready = sem("x2_hi_ready")
        tanh_done = sem("tanh_done")
        exp_done = sem("exp_done")
        mix_ready = sem("mix_ready")
        logits_copied = sem("logits_copied")
        route_exp = sem("route_exp")
        silu_tanh = sem("silu_tanh")
        weights_T_ready = sem("weights_T_ready")
        lora_copied = sem("lora_copied")
        prod_hi_ready = sem("prod_hi_ready")
        idx_step = sem("idx_step")
        zeroed = sem("zeroed")
        soft_dve = sem("soft_dve")
        small_lo_ready = sem("small_lo_ready")
        win_lo_dve = sem("win_lo_dve")
        ffn_lo_dve = sem("ffn_lo_dve")
        embedded = sem("embedded")
        stats1_done = sem("stats1_done")
        stats2_done = sem("stats2_done")
        normed1 = sem("normed1")
        normed2 = sem("normed2")
        x1_lo_ready = sem("x1_lo_ready")
        x2_lo_ready = sem("x2_lo_ready")
        gated = sem("gated")
        clamped = sem("clamped")
        b_ready = sem("b_ready")
        scanned = sem("scanned")
        carried = sem("carried")
        mixed = sem("mixed")
        routed = sem("routed")
        gate_used = sem("gate_used")
        up_used = sem("up_used")
        weighted = sem("weighted")
        finished = sem("finished")
        pool_set = sem("pool_set")
        win_lo_pool = sem("win_lo_pool")
        ffn_lo_pool = sem("ffn_lo_pool")
        latents_split = sem("latents_split")
        x1_ready = sem("x1_ready")
        rstd1_ready = sem("rstd1_ready")
        rstd2_ready = sem("rstd2_ready")
        prod_lo_ready = sem("prod_lo_ready")

        GU, LA, DN = 0, 4096, 4096 + 512
        SCALE_A, SCALE_A2 = 10, 11
        WIN_DVE = 4
        FFN_DVE = 5
        BACK_AFTER, LATENTS_AFTER, TURN_2_AFTER, LAST_EARLY = 3, 5, 6, 2
        ROWS_IN = 16 * TT

        def piece(n):
            return slice(n * PIECE, (n + 1) * PIECE)

        win_stage = [decay[:, 0:2, :], decay[:, 2:4, :], mix[:, 0:2, :], mix[:, 2:4, :]]
        ffn_stage = [chan[:, 2:4, :], prod[:, 0:2, :]]
        ffn_stage += [hidden[:, t:t + 2, :] for t in range(2 * TT, 4 * TT, 2)]
        ffn_stage += [prod[:, 0:2, :]]
        ffn_stage = [s.rearrange("p c t -> p (c t)") for s in ffn_stage]

        def x1_buffers(b):
            return (x2_hi, x2_lo) if isinstance(b, int) and b == 0 else (xg_hi, xg_lo)

        def turn_1_bank(b, j):
            return rows[j - 2] if isinstance(b, int) and b == 0 and j >= 2 else turn[j % 2]

        def win_raw(m):
            return (decay, mix)[m // 4][:, m % 4, :]

        def win_part(w, m):
            return w[:, m, :, :].rearrange("p k f -> p (k f)")

        def gu(w, c, g, k):
            at = GU + ((2 * c + g) * KC + k) * P
            return w[:, at:at + P]

        def register_wait_ends(eng):
            eng.sem_inc(wait_carrier, 1)

        block = ctx.enter_context(nc.Block())

        @block.sync
        def _(sp):
            sp.dma_start(ids_sb[:, :], ids).then_inc(ids_in, 16)
            for n in range(4):
                sp.dma_start(win_stage[n].rearrange("p c t -> p (c t)"),
                             w_in[:, piece(n)]).then_inc(win_in[n], 16)
                if n == 0:
                    sp.dma_start(router_raw[:, :, :], router).then_inc(small_in, 16)
                    sp.dma_start(select_raw, selector).then_inc(small_in, 16)
                    sp.dma_start(rank_sb[:, :, :], rank).then_inc(small_in, 16)
                    sp.wait_ge(text_in_0[1], ROWS_IN // 2)
            sp.wait_ge(text_in, ROWS_IN)
            for n in range(FW // PIECE):
                if n == 1:
                    sp.wait_ge(latents_in, ROWS_IN)
                if n == 6:
                    sp.wait_ge(ffn_lo_dve, 2)
                sp.dma_start(ffn_stage[n], w_ffn[:, piece(n)]).then_inc(ffn_in[n], 16)
            with sp.Fori(0, T // P) as t:
                sp.wait_ge(finished, t + 1)
                sp.dma_start(out[t], hidden[:, t, :]).then_inc(stored, 16)
            sp.wait_ge(stored, 16 * (T // P))

        @block.tensor
        def _(pe):
            def split_product(acc, w_hi, w_lo, x_hi, x_lo, first, last):
                pe.matmul(acc, w_hi, x_hi, start=first, stop=False)
                pe.matmul(acc, w_hi, x_lo, start=False, stop=False)
                return pe.matmul(acc, w_lo, x_hi, start=False, stop=last)

            def keep_warm(n):
                for _ in range(n):
                    pe.transpose(ring[3][:, 0:P], ident[:, :], ident[:, :])

            def turn_latents(b):
                pe.wait_ge(latents_split, 2 * (b + 2))
                for j in range(TT):
                    mm = pe.transpose(turn[1][:, j * P:(j + 1) * P],
                                      latent_parts[:, j, :].bitcast(F32), ident[:, :])
                mm.then_inc(latents_turned, 1)

            def project(b, j):
                pe.wait_ge(latent_T_ready, j // 2 + 1 if isinstance(b, int) and b == 0 else b + 2)
                for t in (j, j + 1):
                    if t >= 2:
                        pe.wait_ge(embedded, TT * b + t - 1)
                    lhs = latent_T[:, t * P:(t + 1) * P]
                    pe.matmul(rows[t % 2][:, :], lhs, proj_hi[:, :], start=True, stop=False)
                    pe.matmul(rows[t % 2][:, :], lhs, proj_lo[:, :], start=False, stop=True)\
                        .then_inc(proj_done, 1)

            def turn_normed(b, j, bank, normed_sem, done):
                pe.wait_ge(normed_sem, TT * b + j + 1)
                for c in range(KC):
                    mm = pe.transpose(bank[:, c * P:(c + 1) * P],
                                      normed[:, j % 2, c * P:(c + 1) * P], ident[:, :])
                mm.then_inc(done, 1)

            def turn_1(b, j):
                if j >= 2 and not (isinstance(b, int) and b == 0):
                    pe.wait_ge(x1_lo_ready, TT * b + j - 1)
                elif j >= 2:
                    pe.wait_ge(embedded, j + 1)
                turn_normed(b, j, turn_1_bank(b, j), normed1, x1_turned)

            def turn_2(b, j, after_latents):
                if j == 0:
                    pe.wait_ge(mixed, TT * (b + 1))
                elif j == 1 and after_latents:
                    pe.wait_ge(latent_T_ready, b + 4)
                elif j >= 2:
                    pe.wait_ge(x2_lo_ready, TT * b + j - 1)
                turn_normed(b, j, turn[j % 2], normed2, x2_turned)

            def turn_back(b, j):
                for t in (j, j + 1):
                    if t == 0:
                        pe.wait_ge(scanned, KC * (b + 1))
                    elif t >= 2:
                        pe.wait_ge(mixed, TT * b + t - 1)
                    for c in range(KC):
                        mm = pe.transpose(turn[(t + 1) % 2][:, c * P:(c + 1) * P],
                                          chan[:, c, t * P:(t + 1) * P], ident[:, :])
                    mm.then_inc(scan_turned, 1)

            def gate(b, m):
                x_hi, x_lo = x1_buffers(b)
                if isinstance(b, int) and b == 0:
                    pe.wait_ge(win_hi_ready, m + 1)
                    if m < WIN_DVE:
                        pe.wait_ge(win_lo_dve, m + 1)
                    else:
                        pe.wait_ge(win_lo_pool, m - WIN_DVE + 1)
                if m >= 4:
                    pe.wait_ge(tanh_done, 2 * KC * b + m - 3)
                elif not (isinstance(b, int) and b == 0):
                    pe.wait_ge(tanh_done, 2 * KC * (b - 1) + m + 5)
                parts = 1 if m else 2
                for h in range(parts):
                    if m == 0:
                        pe.wait_ge(x1_lo_ready, TT * b + (h + 1) * TT // 2)
                    at = slice(h * BT // parts, (h + 1) * BT // parts)
                    for k in range(KC):
                        mm = split_product(ring[m % 4][:, at], win_hi[:, m, k, :],
                                           win_lo[:, m, k, :], x_hi[:, k, at], x_lo[:, k, at],
                                           k == 0, k == KC - 1)
                mm.then_inc(gate_done, 1)

            def gates(b, embed_next):
                early = 0 if embed_next else LAST_EARLY
                for m in range(2 * KC):
                    gate(b, m)
                    if m == BACK_AFTER - early:
                        turn_back(b - 1, 0)
                    if m == BACK_AFTER + 1 - early:
                        turn_back(b - 1, 2)
                    if m == LATENTS_AFTER and embed_next:
                        pe.wait_ge(mixed, TT * b - 1)
                        turn_latents(b + 1)
                    if m == TURN_2_AFTER - early:
                        turn_2(b - 1, 0, embed_next)
                        turn_2(b - 1, 1, embed_next)
                    if m == TURN_2_AFTER + 1 - early:
                        turn_2(b - 1, 2, embed_next)
                        turn_2(b - 1, 3, embed_next)
                if embed_next:
                    project(b + 1, 0)

            def expert(b, c, g, bank):
                for k in range(KC):
                    mm = split_product(ring[bank][:, :], gu(ffn_hi, c, g, k), gu(ffn_lo, c, g, k),
                                       x2_hi[:, k, :], x2_lo[:, k, :], k == 0, k == KC - 1)
                mm.then_inc(expert_done, 1)

            def spread(bank, c):
                pe.matmul(ring[bank][:, :], select[:, c, :], weights_T,
                          start=True, stop=True).then_inc(spread_done, 1)

            def router_logits(b, after_gates):
                if after_gates:
                    pe.wait_ge(tanh_done, 2 * KC * (b + 1) + 5)
                pe.wait_ge(x2_hi_ready, TT * (b + 1))
                for k in range(KC):
                    pe.matmul(ring[0][:, :], router_w[:, k * 2 * E:k * 2 * E + P], x2_hi[:, k, :],
                              start=(k == 0), stop=False)
                pe.wait_ge(x2_lo_ready, TT * (b + 1))
                for k in range(KC):
                    mm = pe.matmul(ring[0][:, :], router_w[:, k * 2 * E:k * 2 * E + P],
                                   x2_lo[:, k, :], start=False, stop=(k == KC - 1))
                mm.then_inc(logits_done, 1)

            def experts(b, after_gates):

                def gate_read(m):
                    if after_gates:
                        pe.wait_ge(tanh_done, 2 * KC * (b + 1) + m + 1)

                gate_read(5)
                expert(b, 0, 0, 1)
                pe.wait_ge(logits_copied, b + 1)
                register_wait_ends(pe)
                for j in range(TT):
                    mm = pe.transpose(turn[0][:, j * 2 * E:(j + 1) * 2 * E],
                                      logits_T[:, j * P:(j + 1) * P], ident[0:2 * E, 0:2 * E])
                mm.then_inc(logits_turned, 1)
                gate_read(6)
                expert(b, 0, 1, 2)
                gate_read(7)
                expert(b, 1, 0, 3)
                expert(b, 1, 1, 0)
                pe.wait_ge(routed, ROUTE * (b + 1))
                register_wait_ends(pe)
                for j in range(TT):
                    mm = pe.transpose(turn[1][0:2 * E, j * P:(j + 1) * P],
                                      route_w[:, j, :].bitcast(F32), ident[:, :])
                mm.then_inc(weights_turned, 1)
                pe.wait_ge(gate_used, KC * b + 1)
                expert(b, 2, 0, 1)
                pe.wait_ge(weights_T_ready, b + 1)
                pe.wait_ge(up_used, KC * b + 1)
                spread(2, 0)
                pe.wait_ge(gate_used, KC * b + 2)
                expert(b, 2, 1, 3)
                pe.wait_ge(up_used, KC * b + 2)
                spread(0, 1)
                pe.wait_ge(weighted, GC * b + 1)
                expert(b, 3, 0, 2)
                pe.wait_ge(gate_used, KC * b + 3)
                expert(b, 3, 1, 1)
                pe.wait_ge(up_used, KC * b + 3)
                spread(3, 2)
                pe.wait_ge(weighted, GC * b + 2)
                for k in range(KC):
                    la = slice(LA + k * P, LA + (k + 1) * P)
                    mm = split_product(ring[0][:, :], ffn_hi[:, la], ffn_lo[:, la],
                                       x2_hi[:, k, :], x2_lo[:, k, :], k == 0, k == KC - 1)
                mm.then_inc(lora_done, 1)
                pe.wait_ge(gate_used, KC * b + 4)
                spread(2, LORA)
                pe.wait_ge(up_used, KC * b + 4)
                spread(1, 3)

            def down_part(b, j, first, last):
                for n in range(first, last):
                    c = ORDER[n]
                    if j == 0:
                        pe.wait_ge(prod_lo_ready, GC * b + n + 1)
                    dn = slice(DN + c * D, DN + (c + 1) * D)
                    mm = split_product(rows[j % 2][:, :], xg_hi[:, c, j * P:(j + 1) * P],
                                       xg_lo[:, c, j * P:(j + 1) * P],
                                       ffn_hi[:, dn], ffn_lo[:, dn], n == 0, n == GC - 1)
                if last == GC:
                    mm.then_inc(down_done, 1)

            def down(b, turn_1_next, turn_last):
                if turn_last:
                    turn_back(b + 1, 0)
                for j in (0, 1):
                    if turn_1_next:
                        pe.wait_ge(embedded, TT * (b + 2) + j + 3)
                    down_part(b, j, 0, 3)
                    if turn_last and j == 0:
                        turn_back(b + 1, 2)
                for j in (0, 1):
                    down_part(b, j, 3, GC)
                if turn_1_next:
                    turn_1(b + 2, 0)
                    turn_1(b + 2, 1)
                if turn_last:
                    turn_2(b + 1, 0, False)
                    turn_2(b + 1, 1, False)
                pe.wait_ge(finished, TT * b + 1)
                down_part(b, 2, 0, GC)
                if turn_1_next:
                    turn_1(b + 2, 2)
                if turn_last:
                    turn_2(b + 1, 2, False)
                    turn_2(b + 1, 3, False)
                pe.wait_ge(finished, TT * b + 2)
                down_part(b, 3, 0, GC)
                if turn_1_next:
                    turn_1(b + 2, 3)

            pe.wait_ge(ident_in, 16)
            for h in range(2):
                pe.wait_ge(latents_split, 2 * (h + 1))
                for j in (2 * h, 2 * h + 1):
                    mm = pe.transpose(turn[h][:, j * P:(j + 1) * P],
                                      latent_parts[:, j, :].bitcast(F32), ident[:, :])
                mm.then_inc(latents_turned, 1)
                if h == 0:
                    pe.wait_ge(proj_hi_ready, 1)
                    pe.wait_ge(small_lo_ready, 1)
                project(0, 2 * h)
            keep_warm(14)
            turn_1(0, 0)
            turn_1(0, 1)
            keep_warm(4)
            turn_1(0, 2)
            turn_1(0, 3)
            gate(0, 0)
            gate(0, 1)
            turn_latents(1)
            gate(0, 2)
            project(1, 0)
            gate(0, 3)
            project(1, 2)
            gate(0, 4)
            gate(0, 5)
            turn_1(1, 0)
            turn_1(1, 1)
            gate(0, 6)
            turn_1(1, 2)
            turn_1(1, 3)
            gate(0, 7)
            pe.wait_ge(ffn_hi_ready, FW // PIECE)
            pe.wait_ge(ffn_lo_dve, FFN_DVE)
            pe.wait_ge(ffn_lo_pool, FW // PIECE - FFN_DVE)
            pe.wait_ge(small_lo_ready, 2)
            pe.wait_ge(select_ready, 1)
            with pe.Fori(0, NB - 2) as i:
                gates(i + 1, True)
                router_logits(i, True)
                project(i + 2, 2)
                experts(i, True)
                down(i, True, False)
            gates(NB - 1, False)
            router_logits(NB - 2, True)
            experts(NB - 2, True)
            down(NB - 2, False, True)
            router_logits(NB - 1, False)
            experts(NB - 1, False)
            down(NB - 1, False, False)

        @block.scalar
        def _(act):
            def high_x(b, j, bank, turned, x_hi, ready):
                act.wait_ge(turned, TT * b + j + 1)
                act.activation(x_hi[:, 0:KC, j * P:(j + 1) * P],
                               bank[:, :].rearrange("p (c t) -> p c t", c=KC),
                               ACT.Copy).then_inc(ready, 1)

            def high_1(b, j):
                high_x(b, j, turn_1_bank(b, j), x1_turned, x1_buffers(b)[0], x1_hi_ready)

            def high_2(b, j):
                high_x(b, j, turn[j % 2], x2_turned, x2_hi, x2_hi_ready)

            def copy_latents(b):
                act.wait_ge(latents_turned, b + 2)
                act.activation(latent_T[:, :], turn[1][:, :], ACT.Copy).then_inc(latent_T_ready, 1)

            def copy_latents_0(h):
                act.wait_ge(latents_turned, h + 1)
                half = slice(h * BT // 2, (h + 1) * BT // 2)
                act.activation(latent_T[:, half], turn[h][:, half], ACT.Copy)\
                    .then_inc(latent_T_ready, 1)

            def gate_tanh(b, m):
                if not (isinstance(b, int) and b == 0):
                    act.wait_ge(scanned, KC * (b - 1) + m // 2 + 1)
                act.wait_ge(gate_done, 2 * KC * b + m + 1)
                act.activation((decay if m % 2 else mix)[:, m // 2, :], ring[m % 4][:, :],
                               ACT.Tanh, scale=0.5).then_inc(tanh_done, 1)

            def decays(b, c):
                act.wait_ge(tanh_done, 2 * KC * b + 2 * c + 2)
                act.wait_ge(gated, KC * b + c + 1)
                act.activation(mix[:, c, :], decay[:, c, :], ACT.Exp,
                               bias=ap_sb[:, SCALE_A2:SCALE_A2 + 1],
                               scale=ap_sb[:, SCALE_A2:SCALE_A2 + 1]).then_inc(exp_done, 1)
                act.activation(decay[:, c, :], decay[:, c, :], ACT.Exp,
                               bias=ap_sb[:, SCALE_A:SCALE_A + 1],
                               scale=ap_sb[:, SCALE_A:SCALE_A + 1]).then_inc(exp_done, 1)

            def roots(b):
                for c in range(KC):
                    act.wait_ge(clamped, KC * b + c + 1)
                    act.activation(mix[:, c, :], mix[:, c, :], ACT.Sqrt, bias=quarter[:, 0:1],
                                   scale=-0.25).then_inc(mix_ready, 1)

            def gates(b, embed_next):
                early = 0 if embed_next else LAST_EARLY
                for m in range(2 * KC):
                    gate_tanh(b, m)
                    if m == LATENTS_AFTER and embed_next:
                        copy_latents(b + 1)
                    if m == TURN_2_AFTER - early:
                        high_2(b - 1, 0)
                        high_2(b - 1, 1)
                        decays(b, 0)
                    if m == TURN_2_AFTER + 1 - early:
                        high_2(b - 1, 2)
                        high_2(b - 1, 3)
                decays(b, 1)
                decays(b, 2)

            def silu(b, c):
                act.wait_ge(expert_done, 2 * KC * b + 2 * c + 1)
                if c == 3:
                    act.wait_ge(prod_lo_ready, GC * b + 1)
                act.activation(prod[:, c % 3, :], ring[(1, 3, 1, 2)[c]][:, :],
                               ACT.Tanh, scale=0.5).then_inc(silu_tanh, 1)

            def high_prod(b, n):
                c = ORDER[n]
                act.wait_ge(weighted, GC * b + n + 1)
                act.activation(xg_hi[:, c, :], prod[:, c % 3, :], ACT.Copy)\
                    .then_inc(prod_hi_ready, 1)

            def experts(b, recur_next):
                act.wait_ge(logits_done, b + 1)
                act.activation(logits_T, ring[0][0:2 * E, :], ACT.Copy)\
                    .then_inc(logits_copied, 1)
                if recur_next:
                    decays(b + 1, KC - 1)
                silu(b, 0)
                act.wait_ge(routed, ROUTE * b + 3)
                act.activation(route[:, 1, :, :], route[:, 0, :, :], ACT.Exp)\
                    .then_inc(route_exp, 1)
                silu(b, 1)
                act.wait_ge(weights_turned, b + 1)
                act.activation(weights_T, turn[1][0:2 * E, :], ACT.Copy)\
                    .then_inc(weights_T_ready, 1)
                if recur_next:
                    roots(b + 1)
                silu(b, 2)
                high_prod(b, 0)
                high_prod(b, 1)
                silu(b, 3)
                high_prod(b, 2)
                act.wait_ge(lora_done, b + 1)
                act.wait_ge(prod_lo_ready, GC * b + 2)
                act.activation(prod[:, LORA % 3, :], ring[0][:, :], ACT.Copy)\
                    .then_inc(lora_copied, 1)
                high_prod(b, 3)
                high_prod(b, 4)

            def high_win(m):
                act.wait_ge(win_in[m // 2], 16)
                act.activation(win_part(win_hi, m), win_raw(m), ACT.Copy)\
                    .then_inc(win_hi_ready, 1)

            def high_ffn(n):
                act.wait_ge(ffn_in[n], 16)
                act.activation(ffn_hi[:, piece(n)], ffn_stage[n], ACT.Copy)\
                    .then_inc(ffn_hi_ready, 1)

            act.dma_start(ap_sb[:, 0:1], a_param).then_inc(a_in, 16)
            act.dma_start(proj_raw, proj).then_inc(proj_in, 16)
            act.dma_start(ident[:, :], identity).then_inc(ident_in, 16)
            act.wait_ge(soft_dve, 2)
            act.activation(ap_sb[:, 3:4], ap_sb[:, 2:3], ACT.Exp).then_inc(soft_act, 1)
            act.wait_ge(soft_dve, 3)
            act.activation(ap_sb[:, 5:6], ap_sb[:, 4:5], ACT.Ln).then_inc(soft_act, 1)
            act.wait_ge(proj_in, 16)
            act.activation(proj_hi[:, :], proj_raw, ACT.Copy).then_inc(proj_hi_ready, 1)
            high_win(0)
            high_win(1)
            copy_latents_0(0)
            copy_latents_0(1)
            act.wait_ge(small_in, 16 * 3)
            act.wait_ge(pool_set, 4)
            act.activation(router_hi_lo[:, :, 0:E], router_raw[:, :, :], ACT.Copy)\
                .then_inc(router_hi_ready, 1)
            act.activation(select[:, :, :].rearrange("p c r -> p (c r)"), select_raw, ACT.Copy)\
                .then_inc(select_ready, 1)
            high_win(2)
            high_win(3)
            high_1(0, 0)
            high_1(0, 1)
            high_win(4)
            high_1(0, 2)
            high_win(5)
            high_1(0, 3)
            high_win(6)
            high_win(7)
            high_ffn(0)
            copy_latents(1)
            act.wait_ge(soft_dve, 13)
            act.wait_ge(win_lo_dve, WIN_DVE)
            act.wait_ge(win_lo_pool, 2 * KC - WIN_DVE)
            gate_tanh(0, 0)
            high_ffn(1)
            high_ffn(2)
            gate_tanh(0, 1)
            high_ffn(3)
            high_ffn(4)
            gate_tanh(0, 2)
            high_ffn(5)
            high_ffn(6)
            gate_tanh(0, 3)
            decays(0, 0)
            gate_tanh(0, 4)
            gate_tanh(0, 5)
            high_1(1, 0)
            high_1(1, 1)
            decays(0, 1)
            gate_tanh(0, 6)
            high_1(1, 2)
            high_1(1, 3)
            decays(0, 2)
            gate_tanh(0, 7)
            decays(0, 3)
            roots(0)
            with act.Fori(0, NB - 2) as i:
                gates(i + 1, True)
                experts(i, True)
                for j in range(TT):
                    high_1(i + 2, j)
            gates(NB - 1, False)
            experts(NB - 2, True)
            for j in range(TT):
                high_2(NB - 1, j)
            experts(NB - 1, False)

        @block.vector
        def _(dve):
            def statistics(b, j, stats, moments, added, done):
                for t in (j, j + 1):
                    dve.wait_ge(added, TT * b + t + 1)
                    register_wait_ends(dve)
                    dve.bn_stats(stats[:, t, :], hidden[:, TT * b + t, :]).then_inc(done, 1)
                for t in (j, j + 1):
                    dve.wait_ge(done, 2 * (TT * b + j) + 1 + t - j)
                    register_wait_ends(dve)
                    dve.bn_aggr(moments[:, t, :], stats[:, t, :]).then_inc(done, 1)

            def embed(b, j):
                if isinstance(b, int) and b == 0:
                    dve.wait_ge(text_in_0[j // 2], ROWS_IN // 2)
                elif j == 0:
                    dve.wait_ge(text_in, ROWS_IN * b)
                for t in (j, j + 1):
                    dve.wait_ge(proj_done, TT * b + t + 1)
                    dve.tensor_tensor(hidden[:, TT * b + t, :], hidden[:, TT * b + t, :],
                                      rows[t % 2][:, :], ALU.add).then_inc(embedded, 1)
                statistics(b, j, stats1, moments1, embedded, stats1_done)

            def mix_in(b, j):
                for t in (j, j + 1):
                    dve.wait_ge(scan_turned, TT * b + t + 1)
                    dve.tensor_tensor(hidden[:, TT * b + t, :], hidden[:, TT * b + t, :],
                                      turn[(t + 1) % 2][:, :], ALU.add).then_inc(mixed, 1)
                statistics(b, j, stats2, moments2, mixed, stats2_done)

            def normalise(b, j, moments, rstd, done):
                dve.tensor_scalar(normed[:, j % 2, :], hidden[:, TT * b + j, :],
                                  moments[:, j, 0:1], rstd[:, j, :], ALU.subtract, ALU.mult)\
                    .then_inc(done, 1)

            def low_x(b, j, bank, x_hi, x_lo, hi_ready, done):
                dve.wait_ge(hi_ready, TT * b + j + 1)
                tok = slice(j * P, (j + 1) * P)
                dve.tensor_tensor(x_lo[:, 0:KC, tok],
                                  bank[:, :].rearrange("p (c t) -> p c t", c=KC),
                                  x_hi[:, 0:KC, tok].bitcast(F32), ALU.subtract)\
                    .then_inc(done, 1)

            def norm_1(b, j):
                first = isinstance(b, int) and b == 0
                if first and j in (0, 2):
                    dve.wait_ge(rstd1_ready, j + 2)
                elif j == 0:
                    dve.wait_ge(rstd1_ready, 2 * (b + 2))
                if j >= 2:
                    dve.wait_ge(x1_turned, TT * b + j - 1)
                normalise(b, j, moments1, rstd1, normed1)

            def low_1(b, j):
                low_x(b, j, turn_1_bank(b, j), *x1_buffers(b), x1_hi_ready, x1_lo_ready)

            def norm_2(b, j):
                if j == 0:
                    dve.wait_ge(rstd2_ready, 2 * (b + 1))
                if j >= 2:
                    dve.wait_ge(x2_turned, TT * b + j - 1)
                normalise(b, j, moments2, rstd2, normed2)

            def low_2(b, j):
                low_x(b, j, turn[j % 2], x2_hi, x2_lo, x2_hi_ready, x2_lo_ready)

            def gate_x(b, c):
                dve.wait_ge(x1_ready, KC * b + c + 1)
                dve.wait_ge(tanh_done, 2 * KC * b + 2 * c + 1)
                dve.scalar_tensor_tensor(chan[:, c, :], mix[:, c, :], 1.0, chan[:, c, :],
                                         ALU.add, ALU.mult).then_inc(gated, 1)

            def clamp(b, c):
                dve.wait_ge(exp_done, 2 * (KC * b + c) + 1)
                dve.tensor_scalar(mix[:, c, :], mix[:, c, :], 1.0, None, ALU.min)\
                    .then_inc(clamped, 1)

            def recur(b, c):
                dve.wait_ge(mix_ready, KC * b + c + 1)
                dve.tensor_tensor(chan[:, c, :], chan[:, c, :], mix[:, c, :], ALU.mult)\
                    .then_inc(b_ready, 1)
                dve.wait_ge(b_ready, KC * b + c + 1)
                if c == 0:
                    dve.wait_ge(carried, b + 1)
                dve.tensor_tensor_scan(chan[:, c, :], decay[:, c, :], chan[:, c, :],
                                       initial=carry[:, c, :], op0=ALU.mult, op1=ALU.add)\
                    .then_inc(scanned, 1)
                if c == KC - 1:
                    dve.wait_ge(scanned, KC * (b + 1))
                    dve.tensor_tensor(carry[:, :, :], chan[:, :, BT - 1:BT],
                                      keep[:, b, :].unsqueeze(2), ALU.mult).then_inc(carried, 1)

            def route_steps(b, first, last):
                s = ROUTE * b
                wide = [TT, E]
                rt = [route[:, n, :, :] for n in range(8)]
                one = [route1[:, n, :, :] for n in range(8)]

                def over(n):
                    return route1[:, n, :, :].to_broadcast([P, *wide])

                def step(n):
                    if first <= n <= last:
                        if n > 1:
                            dve.wait_ge(routed, s + n - 1)
                        return True
                    return False

                if step(1):
                    dve.wait_ge(logits_turned, b + 1)
                    dve.tensor_reduce(rt[0], turn[0][:, 0:TT * 2 * E].rearrange(
                        "p (t h e) -> p t e h", t=TT, h=2), X, ALU.add).then_inc(routed, 1)
                if step(2):
                    dve.tensor_reduce(one[0], rt[0], X, ALU.max).then_inc(routed, 1)
                if step(3):
                    dve.tensor_tensor(rt[0], rt[0], over(0), ALU.subtract).then_inc(routed, 1)
                if step(4):
                    dve.wait_ge(route_exp, b + 1)
                    dve.tensor_reduce(one[1], rt[1], X, ALU.add).then_inc(routed, 1)
                if step(5):
                    dve.reciprocal(one[2], one[1]).then_inc(routed, 1)
                if step(6):
                    dve.tensor_tensor(rt[2], rt[1], over(2), ALU.mult).then_inc(routed, 1)
                for at, src, chosen in ((7, 2, 4), (13, 5, 6)):
                    if step(at):
                        dve.tensor_reduce(one[3], rt[src], X, ALU.max).then_inc(routed, 1)
                    if step(at + 1):
                        dve.tensor_tensor(rt[3], rt[src], over(3), ALU.is_equal)\
                            .then_inc(routed, 1)
                    if step(at + 2):
                        dve.tensor_tensor(rt[3], rt[3], rank_sb[:, :, :], ALU.mult)\
                            .then_inc(routed, 1)
                    if step(at + 3):
                        dve.tensor_reduce(one[4], rt[3], X, ALU.max).then_inc(routed, 1)
                    if step(at + 4):
                        dve.tensor_tensor(rt[chosen], rt[3], over(4), ALU.is_equal)\
                            .then_inc(routed, 1)
                    if at == 7 and step(12):
                        dve.scalar_tensor_tensor(rt[5], rt[4], -2.0, rt[2], ALU.mult, ALU.add)\
                            .then_inc(routed, 1)
                if step(18):
                    dve.tensor_tensor(rt[6], rt[6], rt[4], ALU.add).then_inc(routed, 1)
                if step(19):
                    dve.tensor_tensor(rt[7], rt[6], rt[2], ALU.mult).then_inc(routed, 1)
                if step(20):
                    dve.tensor_copy(route_w[:, :, 0:E], rt[7]).then_inc(routed, 1)
                if step(21):
                    dve.tensor_tensor(route_w[:, :, E:2 * E], rt[7],
                                      route_w[:, :, 0:E].bitcast(F32), ALU.subtract)\
                        .then_inc(routed, 1)

            def silu_up(b, c):
                gate_bank, up_bank = ((1, 2), (3, 0), (1, 3), (2, 1))[c]
                slot = prod[:, c % 3, :]
                dve.wait_ge(silu_tanh, KC * b + c + 1)
                dve.scalar_tensor_tensor(slot, slot, 1.0, ring[gate_bank][:, :],
                                         ALU.add, ALU.mult).then_inc(gate_used, 1)
                dve.wait_ge(gate_used, KC * b + c + 1)
                dve.wait_ge(expert_done, 2 * KC * b + 2 * c + 2)
                dve.tensor_tensor(slot, slot, ring[up_bank][:, :], ALU.mult).then_inc(up_used, 1)

            def weigh(b, n):
                c = ORDER[n]
                slot = prod[:, c % 3, :]
                if c == LORA:
                    dve.wait_ge(lora_copied, b + 1)
                else:
                    dve.wait_ge(up_used, KC * b + c + 1)
                dve.wait_ge(spread_done, GC * b + n + 1)
                dve.tensor_tensor(slot, slot, ring[(2, 0, 3, 2, 1)[n]][:, :], ALU.mult)\
                    .then_inc(weighted, 1)

            def finish(b, j):
                dve.wait_ge(down_done, TT * b + j + 1)
                dve.tensor_tensor(hidden[:, TT * b + j, :], hidden[:, TT * b + j, :],
                                  rows[j % 2][:, :], ALU.add).then_inc(finished, 1)

            def low_win(m):
                dve.wait_ge(win_hi_ready, m + 1)
                dve.tensor_tensor(win_part(win_lo, m), win_raw(m),
                                  win_part(win_hi, m).bitcast(F32), ALU.subtract)\
                    .then_inc(win_lo_dve, 1)

            def low_ffn(n):
                dve.wait_ge(ffn_hi_ready, n + 1)
                dve.tensor_tensor(ffn_lo[:, piece(n)], ffn_stage[n],
                                  ffn_hi[:, piece(n)].bitcast(F32), ALU.subtract)\
                    .then_inc(ffn_lo_dve, 1)

            dve.memset(hidden[:, 0:TT // 2, :], 0.0).then_inc(zeroed, 1)
            dve.wait_ge(ids_in, 16)
            dve.tensor_scalar(idx_tmp[:, 0, :], ids_sb[:, :], 0.0, float(OUT_OF_RANGE),
                              ALU.is_lt, ALU.mult).then_inc(idx_step, 1)
            dve.tensor_scalar(idx_tmp[:, 1, :], ids_sb[:, :], float(VOCAB), float(OUT_OF_RANGE),
                              ALU.is_lt, ALU.mult).then_inc(idx_step, 1)
            dve.tensor_scalar(image_idx[:, :], ids_sb[:, :], float(VOCAB), None, ALU.subtract)\
                .then_inc(idx_step, 1)
            dve.wait_ge(idx_step, 3)
            dve.tensor_tensor(image_idx[:, :], image_idx[:, :], idx_tmp[:, 1, :], ALU.max)\
                .then_inc(idx_step, 1)
            dve.tensor_tensor(text_idx[:, :], ids_sb[:, :], idx_tmp[:, 0, :], ALU.max)\
                .then_inc(idx_step, 1)
            dve.wait_ge(a_in, 16)

            def col(n):
                return ap_sb[:, n:n + 1]

            dve.tensor_scalar(col(1), col(0), -1.0, None, ALU.mult).then_inc(soft_dve, 1)
            dve.wait_ge(soft_dve, 1)
            dve.tensor_tensor(col(2), col(0), col(1), ALU.min).then_inc(soft_dve, 1)
            dve.memset(hidden[:, TT // 2:TT, :], 0.0).then_inc(zeroed, 1)
            dve.wait_ge(soft_act, 1)
            dve.tensor_scalar(col(4), col(3), 1.0, None, ALU.add).then_inc(soft_dve, 1)
            dve.wait_ge(soft_dve, 3)
            dve.tensor_scalar(col(6), col(4), 1.0, None, ALU.subtract).then_inc(soft_dve, 1)
            dve.wait_ge(soft_dve, 4)
            dve.tensor_scalar(col(7), col(6), 0.0, None, ALU.is_equal).then_inc(soft_dve, 1)
            dve.wait_ge(soft_dve, 5)
            dve.tensor_tensor(col(6), col(6), col(7), ALU.add).then_inc(soft_dve, 1)
            dve.wait_ge(soft_act, 2)
            dve.tensor_tensor(col(8), col(5), col(7), ALU.add).then_inc(soft_dve, 1)
            dve.wait_ge(soft_dve, 6)
            dve.reciprocal(col(9), col(6)).then_inc(soft_dve, 1)
            dve.wait_ge(soft_dve, 8)
            dve.tensor_tensor(col(8), col(8), col(9), ALU.mult).then_inc(soft_dve, 1)
            dve.wait_ge(soft_dve, 9)
            dve.tensor_tensor(col(8), col(8), col(3), ALU.mult).then_inc(soft_dve, 1)
            dve.wait_ge(soft_dve, 10)
            dve.scalar_tensor_tensor(col(9), col(0), 0.0, col(8), ALU.max, ALU.add)\
                .then_inc(soft_dve, 1)
            dve.wait_ge(soft_dve, 11)
            dve.tensor_scalar(col(SCALE_A), col(9), -4.0, None, ALU.mult).then_inc(soft_dve, 1)
            dve.tensor_scalar(col(SCALE_A2), col(9), -8.0, None, ALU.mult).then_inc(soft_dve, 1)

            dve.wait_ge(proj_hi_ready, 1)
            dve.tensor_tensor(proj_lo[:, :], proj_raw, proj_hi[:, :].bitcast(F32), ALU.subtract)\
                .then_inc(small_lo_ready, 1)

            def split_first(slot, first, last, there, count):
                at, raw = slice(first, last), latents[:, slot, first:last, :]
                dve.wait_ge(*there)
                if slot:
                    dve.wait_ge(latents_turned, 2)
                dve.tensor_copy(latent_parts[:, at, 0:Q], raw).then_inc(latents_split, 1)
                dve.wait_ge(latents_split, count + 1)
                dve.tensor_tensor(latent_parts[:, at, Q:2 * Q], raw,
                                  latent_parts[:, at, 0:Q].bitcast(F32), ALU.subtract)\
                    .then_inc(latents_split, 1)

            split_first(0, 0, 2, (latents_in_0[0], ROWS_IN // 2), 0)
            low_win(0)
            low_win(1)
            split_first(0, 2, 4, (latents_in_0[1], ROWS_IN // 2), 2)
            embed(0, 0)
            embed(0, 2)
            dve.wait_ge(select_ready, 1)
            norm_1(0, 0)
            norm_1(0, 1)
            norm_1(0, 2)
            low_1(0, 0)
            norm_1(0, 3)
            low_1(0, 1)
            low_1(0, 2)
            low_1(0, 3)
            split_first(1, 0, TT, (latents_in, ROWS_IN), 4)
            for m in range(2, WIN_DVE):
                low_win(m)
            dve.wait_ge(router_hi_ready, 1)
            dve.tensor_tensor(router_hi_lo[:, :, E:2 * E], router_raw[:, :, :],
                              router_hi_lo[:, :, 0:E].bitcast(F32), ALU.subtract)\
                .then_inc(small_lo_ready, 1)
            dve.memset(keep[:, :, :], 1.0).then_inc(zeroed, 1)
            dve.wait_ge(zeroed, 3)
            for b in range(NB):
                if (b + 1) * BT % SEQ == 0:
                    dve.memset(keep[:, b, :], 0.0).then_inc(zeroed, 1)
            dve.memset(carry[:, :, :], 0.0).then_inc(carried, 1)
            low_ffn(0)
            embed(1, 0)
            low_ffn(1)
            embed(1, 2)
            gate_x(0, 0)
            low_ffn(2)
            norm_1(1, 0)
            norm_1(1, 1)
            gate_x(0, 1)
            low_ffn(3)
            clamp(0, 0)
            norm_1(1, 2)
            low_1(1, 0)
            norm_1(1, 3)
            low_1(1, 1)
            low_ffn(4)
            gate_x(0, 2)
            clamp(0, 1)
            low_1(1, 2)
            low_1(1, 3)
            gate_x(0, 3)
            clamp(0, 2)
            clamp(0, 3)
            dve.wait_ge(ffn_lo_pool, FW // PIECE - FFN_DVE)
            dve.memset(hidden[:, 3 * TT:4 * TT, :], 0.0).then_inc(zeroed, 1)
            for c in range(KC):
                recur(0, c)

            def gates(b, embed_next):
                mix_in(b - 1, 0)
                mix_in(b - 1, 2)
                norm_2(b - 1, 0)
                norm_2(b - 1, 1)
                gate_x(b, 0)
                gate_x(b, 1)
                norm_2(b - 1, 2)
                low_2(b - 1, 0)
                norm_2(b - 1, 3)
                low_2(b - 1, 1)
                gate_x(b, 2)
                low_2(b - 1, 2)
                low_2(b - 1, 3)
                if embed_next:
                    embed(b + 1, 0)
                gate_x(b, 3)

            def experts(b, recur_next, embed_next):
                route_steps(b, 1, 3)
                if recur_next:
                    for c in range(KC):
                        clamp(b + 1, c)
                silu_up(b, 0)
                route_steps(b, 4, ROUTE)
                silu_up(b, 1)
                if embed_next:
                    embed(b + 2, 2)
                weigh(b, 0)
                if recur_next:
                    recur(b + 1, 0)
                    recur(b + 1, 1)
                silu_up(b, 2)
                weigh(b, 1)
                if recur_next:
                    recur(b + 1, 2)
                silu_up(b, 3)
                weigh(b, 2)
                if recur_next:
                    recur(b + 1, 3)
                weigh(b, 3)
                weigh(b, 4)

            with dve.Fori(0, NB - 2) as i:
                gates(i + 1, True)
                experts(i, True, True)
                norm_1(i + 2, 0)
                norm_1(i + 2, 1)
                finish(i, 0)
                finish(i, 1)
                norm_1(i + 2, 2)
                low_1(i + 2, 0)
                norm_1(i + 2, 3)
                low_1(i + 2, 1)
                finish(i, 2)
                low_1(i + 2, 2)
                finish(i, 3)
                low_1(i + 2, 3)
            gates(NB - 1, False)
            experts(NB - 2, True, False)
            mix_in(NB - 1, 0)
            mix_in(NB - 1, 2)
            norm_2(NB - 1, 0)
            norm_2(NB - 1, 1)
            finish(NB - 2, 0)
            finish(NB - 2, 1)
            norm_2(NB - 1, 2)
            low_2(NB - 1, 0)
            norm_2(NB - 1, 3)
            low_2(NB - 1, 1)
            finish(NB - 2, 2)
            low_2(NB - 1, 2)
            low_2(NB - 1, 3)
            finish(NB - 2, 3)
            experts(NB - 1, False, False)
            for j in range(TT):
                finish(NB - 1, j)

        @block.gpsimd
        def _(pool):
            def gather(b, idx, table, rows_of, dst, done, tiles=range(TT)):
                if b > 1:
                    pool.wait_ge(done, ROWS_IN * (b - 1))
                for j in tiles:
                    t = TT * b + j
                    pool.indirect_dma_start(
                        out=dst(j), out_offset=None, in_=table,
                        in_offset=bass.IndirectOffsetOnAxis(ap=idx[:, t:t + 1], axis=0),
                        bounds_check=rows_of - 1, oob_is_err=False).then_inc(done, 16)

            def gather_text(b, done=text_in, tiles=range(TT)):
                gather(b, text_idx, tok_emb, VOCAB, lambda j: hidden[:, TT * b + j, :], done, tiles)

            def gather_latents(b, done=latents_in, tiles=range(TT)):
                gather(b, image_idx, codebook, VQ, lambda j: latents[:, b % 2, j, :], done, tiles)

            def split_latents(b, slot):
                pool.wait_ge(latents_in, ROWS_IN * b)
                pool.wait_ge(latents_turned, b + 1)
                register_wait_ends(pool)
                raw = latents[:, slot, :, :]
                pool.tensor_copy(latent_parts[:, :, 0:Q], raw).then_inc(latents_split, 1)
                pool.wait_ge(latents_split, 2 * b + 3)
                register_wait_ends(pool)
                pool.tensor_tensor(latent_parts[:, :, Q:2 * Q], raw,
                                   latent_parts[:, :, 0:Q].bitcast(F32), ALU.subtract)\
                    .then_inc(latents_split, 1)

            def inverse_std(b, moments, rstd, stats_done, done, count, first=0, last=TT):
                pool.wait_ge(stats_done, 2 * (TT * b + last))
                register_wait_ends(pool)
                pool.tensor_scalar(rstd[:, first:last, :], moments[:, first:last, 1:2], EPS, None,
                                   ALU.add).then_inc(done, 1)
                pool.wait_ge(done, count + 1)
                pool.tensor_tensor(rstd[:, first:last, :], rstd[:, first:last, :],
                                   minus_half[:, first:last, :], ALU.pow).then_inc(done, 1)

            def whole_x(b, c):
                x_hi, x_lo = x1_buffers(b)
                if c == 0:
                    pool.wait_ge(x1_lo_ready, TT * (b + 1))
                    if not (isinstance(b, int) and b == 0):
                        pool.wait_ge(scan_turned, TT * b)
                pool.tensor_tensor(chan[:, c, :], x_hi[:, c, :].bitcast(F32),
                                   x_lo[:, c, :].bitcast(F32), ALU.add).then_inc(x1_ready, 1)

            def gates(b):
                inverse_std(b - 1, moments2, rstd2, stats2_done, rstd2_ready, 2 * (b - 1))
                for c in range(KC):
                    whole_x(b, c)

            def experts(b, embed_next):
                if embed_next:
                    inverse_std(b + 2, moments1, rstd1, stats1_done, rstd1_ready, 2 * (b + 3))
                for n, c in enumerate(ORDER):
                    pool.wait_ge(prod_hi_ready, GC * b + n + 1)
                    pool.tensor_tensor(xg_lo[:, c, :], prod[:, c % 3, :],
                                       xg_hi[:, c, :].bitcast(F32), ALU.subtract)\
                        .then_inc(prod_lo_ready, 1)

            def low_win(m):
                pool.wait_ge(win_hi_ready, m + 1)
                pool.tensor_tensor(win_part(win_lo, m), win_raw(m),
                                   win_part(win_hi, m).bitcast(F32), ALU.subtract)\
                    .then_inc(win_lo_pool, 1)

            def low_ffn(n):
                pool.wait_ge(ffn_hi_ready, n + 1)
                pool.tensor_tensor(ffn_lo[:, piece(n)], ffn_stage[n],
                                   ffn_hi[:, piece(n)].bitcast(F32), ALU.subtract)\
                    .then_inc(ffn_lo_pool, 1)

            pool.memset(latents[:, :, :, :], 0.0).then_inc(pool_set, 1)
            pool.memset(quarter[:, :], 0.25).then_inc(pool_set, 1)
            pool.memset(minus_half[:, :, :], -0.5).then_inc(pool_set, 1)
            pool.memset(router_w[:, :].bitcast(F32), 0.0).then_inc(pool_set, 1)
            pool.memset(hidden[:, TT:2 * TT, :], 0.0).then_inc(pool_set, 1)
            pool.wait_ge(pool_set, 1)
            pool.wait_ge(idx_step, 4)
            for h in range(2):
                half = (2 * h, 2 * h + 1)
                gather_latents(0, latents_in_0[h], half)
                pool.wait_ge(zeroed, h + 1)
                pool.wait_ge(idx_step, 5)
                gather_text(0, text_in_0[h], half)
            pool.wait_ge(pool_set, 5)
            gather_text(1)
            pool.wait_ge(pool_set, 3)
            inverse_std(0, moments1, rstd1, stats1_done, rstd1_ready, 0, 0, 2)
            inverse_std(0, moments1, rstd1, stats1_done, rstd1_ready, 2, 2, 4)
            gather_latents(1)
            for m in range(WIN_DVE, 2 * KC):
                low_win(m)
            pool.wait_ge(latents_split, 6)
            pool.memset(latents[:, :, :, :], 0.0).then_inc(pool_set, 1)
            pool.wait_ge(small_lo_ready, 1)
            whole_x(0, 0)
            whole_x(0, 1)
            pool.wait_ge(pool_set, 6)
            gather_latents(2)
            inverse_std(1, moments1, rstd1, stats1_done, rstd1_ready, 4)
            pool.wait_ge(ffn_lo_dve, 1)
            whole_x(0, 2)
            whole_x(0, 3)
            for n in range(FFN_DVE, FW // PIECE):
                low_ffn(n)
            gather_latents(3)
            pool.wait_ge(ffn_lo_dve, FFN_DVE - 1)
            pool.memset(hidden[:, 2 * TT:3 * TT, :], 0.0).then_inc(pool_set, 1)
            pool.wait_ge(pool_set, 7)
            gather_text(2)
            pool.wait_ge(zeroed, 4 + NB * BT // SEQ)
            gather_text(3)
            with pool.Fori(0, NB - 2) as i:
                split_latents(i + 2, i)
                gates(i + 1)
                experts(i, True)
            gates(NB - 1)
            experts(NB - 2, False)
            inverse_std(NB - 1, moments2, rstd2, stats2_done, rstd2_ready, 2 * (NB - 1))
            experts(NB - 1, False)



def kernel(x, L0_tok_tok_emb, L0_tok_codebook, L0_tok_proj_w, L0_attn_W_in, L0_attn_a_param,
           L0_ffn_G, L0_ffn_gate_w, L0_ffn_up_w, L0_ffn_down_w, L0_ffn_lora_A, L0_ffn_lora_B):
    import numpy as np
    from concourse import bacc
    from concourse.bass_utils import run_bass_kernel_spmd

    def chunks(w):
        return np.asarray(w).reshape(-1, P, KC, P).transpose(3, 0, 2, 1)

    w_in = chunks(L0_attn_W_in).reshape(P, 2, KC, KC * P).transpose(0, 2, 1, 3)
    gate, up = (chunks(np.asarray(w).reshape(E * F, D)) for w in (L0_ffn_gate_w, L0_ffn_up_w))
    lora_a = chunks(np.asarray(L0_ffn_lora_A).reshape(E * R, D))
    down = np.asarray(L0_ffn_down_w).transpose(0, 2, 1).reshape(KC, P, D).transpose(1, 0, 2)
    lora_b = np.asarray(L0_ffn_lora_B).transpose(0, 2, 1).reshape(P, D)
    proj = np.asarray(L0_tok_proj_w).T
    selector = np.zeros((2 * E, GC, P), np.float32)
    for r in range(P):
        for half in range(2):
            for c in range(KC):
                selector[half * E + (P * c + r) // F, c, r] = 0.5
            selector[half * E + r // R, LORA, r] = 1.0
    arrays = {
        "ids": np.asarray(x).reshape(T // P, P).T,
        "tok_emb": np.asarray(L0_tok_tok_emb),
        "codebook": np.asarray(L0_tok_codebook),
        "proj": np.concatenate([proj, proj]),
        "w_in": w_in.reshape(P, 2 * KC * D),
        "a_param": np.asarray(L0_attn_a_param).reshape(P, 1),
        "router": np.asarray(L0_ffn_G).reshape(KC, P, E).transpose(1, 0, 2),
        "w_ffn": np.concatenate([np.stack([gate, up], 2).reshape(P, -1), lora_a.reshape(P, -1),
                                 down.reshape(P, -1), lora_b], 1),
        "identity": np.eye(P, dtype=np.float32),
        "selector": selector,
        "rank": np.broadcast_to(np.arange(E, 0, -1, dtype=np.float32), (P, TT, E)),
    }
    nc = bacc.Bacc("TRN2", target_bir_lowering=False, num_devices=1)
    args = {}
    for name, a in arrays.items():
        arrays[name] = a = np.ascontiguousarray(a)
        args[name] = nc.dram_tensor(name, a.shape, mybir.dt.from_np(a.dtype),
                                    kind="ExternalInput").ap()
    out = nc.dram_tensor("out", (T // P, P, D), F32, kind="ExternalOutput").ap()
    tower_program(nc, **args, out=out)
    result = run_bass_kernel_spmd(nc, [arrays], core_ids=[0])
    return result.results[0]["out"].reshape(2, SEQ, D)
```
